# Optimizing a Trainium2 kernel written in Bass

```python
import numpy as np
import jax
import jax.numpy as jnp

def _softmax(x, axis=-1):
    return jax.nn.softmax(x, axis=axis)

def _gelu(x):
    return jax.nn.gelu(x, approximate=True)

def _silu(x):
    return jax.nn.silu(x)

def _sigmoid(x):
    return jax.nn.sigmoid(x)

def _layernorm(x, axis=-1, eps=1e-05):
    m = jnp.mean(x, axis=axis, keepdims=True)
    v = jnp.var(x, axis=axis, keepdims=True)
    return (x - m) / jnp.sqrt(v + eps)

def _scatter_add(tgt, idx, src, axis=0):
    return tgt.at[idx].add(src)

def _segment_sum(src, seg, n):
    return jax.ops.segment_sum(src, seg, n)
kernel_name = 'mk_adaln_ffn_d1_seqx_r2_6c5863'

def setup_inputs(seed: int=0):
    np.random.seed(seed)
    _w = jnp.asarray

    def _rec_inputs():
        import jax
        import jax.numpy as jnp
        _rk = jax.random.key(seed)
        x = -0.000125 + 0.9999 * jax.random.normal(jax.random.fold_in(_rk, 1), (8, 512, 2048), jnp.float32)
        _lenS = 512 - jax.random.randint(jax.random.fold_in(_rk, 7), (8,), 0, max(1, 512 // 4) + 1, jnp.int32)
        _lenS2 = 512 - jax.random.randint(jax.random.fold_in(_rk, 8), (8,), 0, max(1, 512 // 4) + 1, jnp.int32)
        itok_B_3_7 = jax.random.randint(jax.random.fold_in(_rk, 11), (8,), 3, 8, jnp.int32)
        return (x, itok_B_3_7)
    x, itok_B_3_7 = _rec_inputs()

    def _L0_cond_setup():
        import jax, jax.numpy as jnp
        import numpy as np
        RANK = 16
        ALPHA = 16.0
        SCALING = ALPHA / RANK
        N_ADAPTERS = 8
        IN_F = 2048
        OUT_F = 2048
        BATCH = 4
        SEQ = 1024
        key = jax.random.key(seed)
        kx, ka, kb, ki = jax.random.split(key, 4)
        x = jax.random.normal(kx, (BATCH, SEQ, IN_F), dtype=jnp.float32)
        A = jax.random.normal(ka, (N_ADAPTERS, OUT_F, RANK), dtype=jnp.float32) * 0.02
        B = jax.random.normal(kb, (N_ADAPTERS, RANK, IN_F), dtype=jnp.float32) * 0.02
        adapter_ids = jax.random.randint(ki, (BATCH,), 0, N_ADAPTERS, dtype=jnp.int32)
        return {'x': x, 'A': A, 'B': B, 'adapter_ids': adapter_ids}
    _L0_cond_all = _L0_cond_setup()
    _L0_cond_in = {k: v for k, v in _L0_cond_all.items() if k in ('A', 'B')}
    del _L0_cond_all

    def _L0_ffn_setup():
        import jax, jax.numpy as jnp
        import numpy as np
        import math
        B, S, IN, OUT = (4, 1024, 2048, 2048)
        E, R, K = (8, 64, 128)
        SCALE = 64.0 / 64.0
        MULTIPLIER = 1.0
        key = jax.random.key(seed)
        ks = jax.random.split(key, 6)
        return {'x': jax.random.normal(ks[0], (B, S, IN), jnp.float32), 'W_org': jax.random.normal(ks[1], (OUT, IN), jnp.float32) * 0.02, 'lora_down': jax.random.normal(ks[2], (E, IN, R), jnp.float32) * 0.02, 'lora_up': jax.random.normal(ks[3], (E, R, OUT), jnp.float32) * 0.02, 'lora_keys': jax.random.normal(ks[4], (E, K), jnp.float32), 'Wq': jax.random.normal(ks[5], (K, IN), jnp.float32) * 0.02}
    _L0_ffn_all = _L0_ffn_setup()
    _L0_ffn_in = {k: v for k, v in _L0_ffn_all.items() if k in ('W_org', 'lora_down', 'lora_up', 'lora_keys', 'Wq')}
    del _L0_ffn_all
    return {'x': x, 'itok_B_3_7': itok_B_3_7, 'L0_cond_A': _L0_cond_in['A'], 'L0_cond_B': _L0_cond_in['B'], 'L0_ffn_W_org': _L0_ffn_in['W_org'], 'L0_ffn_lora_down': _L0_ffn_in['lora_down'], 'L0_ffn_lora_up': _L0_ffn_in['lora_up'], 'L0_ffn_lora_keys': _L0_ffn_in['lora_keys'], 'L0_ffn_Wq': _L0_ffn_in['Wq']}

def reference(x, itok_B_3_7, L0_cond_A, L0_cond_B, L0_ffn_W_org, L0_ffn_lora_down, L0_ffn_lora_up, L0_ffn_lora_keys, L0_ffn_Wq):
    import jax
    import jax.numpy as jnp

    def _L0_cond_ref(x, A, B, adapter_ids):
        import jax, jax.numpy as jnp
        import numpy as np
        RANK = 16
        ALPHA = 16.0
        SCALING = ALPHA / RANK
        N_ADAPTERS = 8
        IN_F = 2048
        OUT_F = 2048
        BATCH = 4
        SEQ = 1024
        B_sel = B[adapter_ids]
        A_sel = A[adapter_ids]
        Bx = jnp.einsum('bni,bri->bnr', x, B_sel)
        out = jnp.einsum('bnr,bor->bno', Bx, A_sel)
        return out * SCALING

    def _L0_ffn_ref(x, W_org, lora_down, lora_up, lora_keys, Wq):
        import jax, jax.numpy as jnp
        import numpy as np
        import math
        B, S, IN, OUT = (4, 1024, 2048, 2048)
        E, R, K = (8, 64, 128)
        SCALE = 64.0 / 64.0
        MULTIPLIER = 1.0
        base = jnp.einsum('bsi,oi->bso', x, W_org)
        q = jnp.einsum('bi,ki->bk', x.mean(axis=1), Wq)
        scores = jnp.einsum('bk,ek->be', q, lora_keys) / math.sqrt(K)
        coeffs = jax.nn.softmax(scores, axis=-1)
        h = jnp.einsum('bsi,eir->bser', x, lora_down)
        delta = jnp.einsum('be,bser,ero->bso', coeffs, h, lora_up)
        return base + delta * (SCALE * MULTIPLIER)
    x = x + _L0_ffn_ref(_L0_cond_ref(x, L0_cond_A, L0_cond_B, itok_B_3_7), L0_ffn_W_org, L0_ffn_lora_down, L0_ffn_lora_up, L0_ffn_lora_keys, L0_ffn_Wq)
    return x

_drawn_inputs = setup_inputs


def setup_inputs(seed=0):
    import zlib

    import numpy as np

    out = dict(_drawn_inputs(seed))
    spreads = {}
    factors = {'L0_ffn_lora_down': 8.0, 'L0_ffn_lora_up': 8.0, 'L0_ffn_lora_keys': 8.0, 'L0_ffn_Wq': 8.0}
    for name, (base, spread) in spreads.items():
        noise = np.random.default_rng([zlib.crc32(name.encode()), seed]).standard_normal(out[name].shape)
        drawn = base * np.exp(spread * noise) if base else spread * noise
        out[name] = jnp.asarray(drawn.astype(out[name].dtype))
    for name, factor in factors.items():
        out[name] = (out[name] * factor).astype(out[name].dtype)
    return out
```

```python
import concourse.bass as bass
from concourse import mybir
from contextlib import ExitStack

F32 = mybir.dt.float32
BF16 = mybir.dt.bfloat16
ALU = mybir.AluOpType
ACT = mybir.ActivationFunctionType
AX = mybir.AxisListType

P = 128
PRODUCTS = ((0, 0), (0, 1), (1, 0), (0, 2), (2, 0), (1, 1), (1, 2), (2, 1))


def lora_ffn(nc, x, ids, a_tab, b_tab, w_cat, up, keys_t, ident, sel_x, sel_m, y):
    NB, _, _, S = x.shape
    C = x.shape[2]
    R = a_tab.shape[3]
    O = up.shape[2]
    ER = w_cat.shape[2] - O - P
    KE = ER // P
    E = keys_t.shape[1]
    K = keys_t.shape[0]
    NA = a_tab.shape[0]
    PAIRS = NB // 2
    OJ = O // S
    CW = w_cat.shape[2]
    WCH = 2
    WP = C // WCH
    WRING = 3
    XP = 4
    XC = C // XP
    LAST = PAIRS - 1
    SCORE_SCALE = 1.0 / (S * float(K) ** 0.5)
    NPROD = len(PRODUCTS)
    assert NPROD * R == P and 2 * R * OJ == P and E // 2 == KE

    ctx = ExitStack()
    with ctx:
        def sb(name, shape, dt):
            return ctx.enter_context(nc.sbuf_tensor(name, shape, dt))

        def pb(name, shape, dt=F32):
            return ctx.enter_context(nc.psum_tensor(name, shape, dt))

        def sem(name):
            return ctx.enter_context(nc.semaphore(name))

        xs = sb("xs", [P, 4 * C * S], F32)
        xv = xs[:, :].rearrange("p (s c t) -> p s c t", s=4, c=C)
        up_sb = sb("up_sb", [P, KE, O], F32)
        pw = sb("pw", [P, PAIRS, S], F32)
        gt = sb("gt", [P, KE, NB * R], F32)
        b_all = sb("b_all", [P, NB, C * R], F32)
        b_cur = [sb(f"b_cur{i}", [P, C * R], F32) for i in range(2)]
        scratch = sb("scratch", [P, C * P], F32)
        a_ord = scratch[:, :].rearrange("p (c m) -> p c m", c=C)
        m_slots = [scratch[:, i * C * P // 2:(i + 1) * C * P // 2].bitcast(BF16) for i in range(2)]
        x_part = [[sb(f"x_part{i}_{k}", [R, S], BF16) for k in range(3)] for i in range(2)]
        x_rest = sb("x_rest", [R, S], F32)
        x_slots = [sb(f"x_slots{i}", [P, S], BF16) for i in range(2)]
        m_rest = sb("m_rest", [P, S], F32)
        m_part = [sb(f"m_part{k}", [P, S], BF16) for k in range(3)]
        g_scaled = sb("g_scaled", [P, KE, 2, R], F32)
        selx_sb = sb("selx_sb", [R, 3, P], BF16)
        selm_sb = sb("selm_sb", [P, 3, 2, P], BF16)
        ident_sb = m_part[0][:, :].bitcast(F32)[:, 0:P]
        wat_sb = m_part[1][:, :].bitcast(F32)[:, 0:NB * R]
        keys_sb = sb("keys_sb", [P, E], F32)
        ka = sb("ka", [R, NB, E], F32)
        ones = sb("ones", [R, P], F32)
        x_sum = [sb(f"x_sum{i}", [R, 1], F32) for i in range(2)]
        sum_wide = [sb(f"sum_wide{i}", [R, P], F32) for i in range(2)]
        smax = sb("smax", [P, 2], F32)
        sdif = sb("sdif", [P, 2, E], F32)
        sexp = sb("sexp", [P, 2, E], F32)
        ssum = sb("ssum", [P, 2], F32)
        srec = sb("srec", [P, 2], F32)
        coef = sdif

        a_raw = xs[:, C * S:C * S + NB * C * R].rearrange("p (b c r) -> p b c r", b=NB, c=C)
        w_ring = xs[:, 2 * C * S:2 * C * S + WRING * WCH * CW].rearrange(
            "p (n c m) -> p n c m", n=WRING, c=WCH)

        bx_ps = [pb(f"bx_ps{i}", [P, S]) for i in range(2)]
        m_ps = pb("m_ps", [P, S])
        sel_ps = [pb(f"sel_ps{i}", [P, S]) for i in range(2)]
        y_ps = [pb(f"y_ps{i}", [P, S]) for i in range(3)]
        NY = len(y_ps)
        p_ps = [y_ps[0], y_ps[1], y_ps[2], sel_ps[0]]
        g_ps, wat_ps = sel_ps[1], m_ps

        const_in = sem("const_in")
        a_in = sem("a_in")
        b_in = sem("b_in")
        up_in = sem("up_in")
        w_in = [sem(f"w_in{i}") for i in range(WRING)]
        x_in = [[sem(f"x_in{i}_{k}") for k in range(XP)] for i in range(2)]
        stored = [[sem(f"stored{i}_{k}") for k in range(XP)] for i in range(2)]
        ones_set = sem("ones_set")
        a_ordered = sem("a_ordered")
        w_used = sem("w_used")
        g_copied = sem("g_copied")
        wat_copied = sem("wat_copied")
        pw_act = sem("pw_act")
        pw_dve = sem("pw_dve")
        gt_mm = sem("gt_mm")
        ka_mm = sem("ka_mm")
        gt_copied = sem("gt_copied")
        ka_copied = sem("ka_copied")
        b_ready = [sem(f"b_ready{i}") for i in range(2)]
        bx_done = [sem(f"bx_done{i}") for i in range(2)]
        x1_done = [sem(f"x1_done{i}") for i in range(2)]
        wide_done = [sem(f"wide_done{i}") for i in range(2)]
        xr_done = [sem(f"xr_done{i}") for i in range(2)]
        x2_done = [sem(f"x2_done{i}") for i in range(2)]
        x3_done = [sem(f"x3_done{i}") for i in range(2)]
        xsel_mm = [sem(f"xsel_mm{i}") for i in range(2)]
        x_slots_done = [sem(f"x_slots_done{i}") for i in range(2)]
        scores_mm = sem("scores_mm")
        max_done = sem("max_done")
        dif_done = sem("dif_done")
        exp_done = sem("exp_done")
        sum_done = sem("sum_done")
        rec_done = sem("rec_done")
        coef_done = sem("coef_done")
        g_scaled_done = sem("g_scaled_done")
        delta_mm = sem("delta_mm")
        mf_done = sem("mf_done")
        m1_done = sem("m1_done")
        mr_done = sem("mr_done")
        m2_done = sem("m2_done")
        m3_done = sem("m3_done")
        msel_mm = sem("msel_mm")
        m_slots_done = sem("m_slots_done")
        y_mm = sem("y_mm")
        y_added = sem("y_added")

        block = ctx.enter_context(nc.Block())

        def slot_of(pair, i):
            return (pair % 2) * 2 + i

        def chunks(pair, i, c, n=1):
            return xs[:, bass.ds((slot_of(pair, i) * C + c) * S, n * S)]

        @block.sync
        def _(sp):
            def load_x(pair, i):
                for k in range(XP):
                    sp.dma_start(chunks(pair, i, k * XC, XC),
                                 x_rows(x, pair, i, k)).then_inc(x_in[i][k], 16)

            def x_rows(t, pair, i, k):
                return t[bass.ds(pair * 2 + i, 1), :, k * XC:(k + 1) * XC, :].rearrange(
                    "b p c t -> (b p) (c t)")

            adapter = [sp.value_load(ids[0:1, b:b + 1], min_val=0, max_val=NA - 1) for b in range(NB)]
            for b in range(NB):
                sp.dma_start(a_raw[:, b, :, :].rearrange("p c r -> p (c r)"),
                             a_tab[bass.ds(adapter[b], 1), :, :, :].rearrange("a p c r -> (a p) (c r)")
                             ).then_inc(a_in, 16)

            def load_w(n):
                sp.dma_start(w_ring[:, n % WRING, :, :].rearrange("p c m -> p (c m)"),
                             w_cat[:, n * WCH:(n + 1) * WCH, :].rearrange("p c m -> p (c m)")
                             ).then_inc(w_in[n % WRING], 16)

            load_w(0)
            for dst, src in ((ident_sb, ident), (keys_sb[:, :], keys_t),
                             (selx_sb[:, :, :], sel_x), (selm_sb[:, :, :, :], sel_m)):
                sp.dma_start(dst, src).then_inc(const_in, 16)
            for b in range(NB):
                sp.dma_start(b_all[:, b, :],
                             b_tab[bass.ds(adapter[b], 1), :, :, :].rearrange("a p c r -> (a p) (c r)")
                             ).then_inc(b_in, 16)
            for n in range(1, WP):
                if n >= WRING:
                    sp.wait_ge(w_used, n - WRING + 1)
                load_w(n)
            load_x(0, 0)
            sp.wait_ge(a_ordered, NB)
            load_x(0, 1)
            sp.dma_start(up_sb[:, :, :], up).then_inc(up_in, 16)
            sp.wait_ge(w_used, WP)
            for i in range(2):
                for k in range(XP):
                    sp.wait_ge(x_in[i][k], 16)
                load_x(1, i)

            def store(pair, i, k):
                sp.wait_ge(y_added, pair * (2 * C) + (i * C + (k + 1) * XC))
                sp.dma_start(x_rows(y, pair, i, k), chunks(pair, i, k * XC, XC)).then_inc(stored[i][k], 16)

            def reload(pair, i, k):
                sp.wait_ge(stored[i][k], pair * 16 + 16)
                sp.wait_ge(x_in[i][k], pair * 16 + 32)
                sp.dma_start(chunks(pair, i, k * XC, XC),
                             x_rows(x, pair + 2, i, k)).then_inc(x_in[i][k], 16)

            for g in range(PAIRS):
                for k in range(XP):
                    store(g, 0, k)
                for k in range(XP):
                    store(g, 1, k)
                    if g < PAIRS - 2:
                        reload(g, 0, k)
                if g < PAIRS - 2:
                    for k in range(XP):
                        reload(g, 1, k)
            for i in range(2):
                for k in range(XP):
                    sp.wait_ge(stored[i][k], 16 * PAIRS)

        @block.tensor
        def _(pe):
            pe.wait_ge(a_ordered, NB)
            for n in range(WP):
                pe.wait_ge(w_in[n % WRING], 16 * (n // WRING + 1))
                for cc in range(WCH):
                    c = n * WCH + cc
                    w = w_ring[:, n % WRING, cc, :]
                    on = dict(start=(c == 0), stop=(c == C - 1))
                    for j in range(OJ):
                        nc.tensor.matmul(p_ps[j][:, :], a_ord[:, c, :], w[:, j * S:(j + 1) * S], **on)
                    nc.tensor.matmul(g_ps[:, :], a_ord[:, c, :], w[:, O:O + ER], **on)
                    last = nc.tensor.matmul(wat_ps[:, 0:NB * R], w[:, O + ER:CW], a_ord[:, c, :], **on)
                last.then_inc(w_used, 1)

            def bx(pair, i, first, end):
                if first == 0:
                    pe.wait_ge(b_ready[i], pair + 1)
                for c in range(first, end):
                    if c % XC == 0:
                        pe.wait_ge(x_in[i][c // XC], pair * 16 + 16)
                    mm = nc.tensor.matmul(bx_ps[i][0:R, :], b_cur[i][:, c * R:(c + 1) * R],
                                          chunks(pair, i, c), start=(c == 0), stop=(c == C - 1))
                if end == C:
                    mm.then_inc(bx_done[i], 1)

            bx(0, 0, 0, C)
            pe.wait_ge(const_in, 16 * 4)
            pe.wait_ge(g_copied, 1)
            for k in range(KE):
                mm = nc.tensor.transpose(g_ps[:, k * P:(k + 1) * P], m_rest[:, k * P:(k + 1) * P],
                                         ident_sb)
            mm.then_inc(gt_mm, 1)
            pe.wait_ge(wat_copied, 1)
            for b in range(NB):
                mm = nc.tensor.matmul(wat_ps[0:R, b * E:(b + 1) * E], wat_sb[:, b * R:(b + 1) * R],
                                      keys_sb[:, :], start=True, stop=True)
            mm.then_inc(ka_mm, 1)
            bx(0, 1, 0, C)
            pe.wait_ge(pw_act, 2 * PAIRS)
            pe.wait_ge(pw_dve, 2 * PAIRS)
            pe.wait_ge(gt_copied, 1)
            pe.wait_ge(ka_copied, 1)
            pe.wait_ge(up_in, 16)

            def select_x(pair, i):
                pe.wait_ge(x3_done[i], pair + 1)
                for k in range(3):
                    mm = nc.tensor.matmul(sel_ps[i][:, :], selx_sb[:, k, :], x_part[i][k][:, :],
                                          start=(k == 0), stop=(k == 2))
                mm.then_inc(xsel_mm[i], 1)

            def scores(pair):
                for i in range(2):
                    pe.wait_ge(wide_done[i], pair + 1)
                    mm = nc.tensor.matmul(m_ps[:, i * E:(i + 1) * E], sum_wide[i][:, :],
                                          ka[:, bass.ds(pair * 2 + i, 1), :].rearrange("r b e -> r (b e)"),
                                          start=True, stop=True)
                mm.then_inc(scores_mm, 1)

            def delta(pair):
                pe.wait_ge(g_scaled_done, pair * 2 + 2)
                for k in range(KE):
                    for j in range(OJ):
                        mm = nc.tensor.matmul(m_ps[2 * R * j:2 * R * (j + 1), :],
                                              g_scaled[:, k, :, :].rearrange("p i r -> p (i r)"),
                                              up_sb[:, k, j * S:(j + 1) * S],
                                              start=(k == 0), stop=(k == KE - 1))
                mm.then_inc(delta_mm, 1)

            def select_m(pair):
                pe.wait_ge(m3_done, pair + 1)
                for i in range(2):
                    for j in range(OJ):
                        n = i * OJ + j
                        if n < 2:
                            pe.wait_ge(x_slots_done[n], pair + 1)
                        else:
                            pe.wait_ge(m_slots_done, pair * 2 * OJ + n - 1)
                        for k in range(3):
                            rows = slice(2 * R * j, 2 * R * (j + 1))
                            mm = nc.tensor.matmul(sel_ps[n % 2][:, :], selm_sb[rows, k, i, :],
                                                  m_part[k][rows, :], start=(k == 0), stop=(k == 2))
                        mm.then_inc(msel_mm, 1)

            def update(pair, n):
                i, c = n // C, n % C
                if c % 4 == 0:
                    pe.wait_ge(m_slots_done, pair * 2 * OJ + i * OJ + c // 4 + 1)
                if n >= NY:
                    pe.wait_ge(y_added, pair * 2 * C + n - NY + 1)
                nc.tensor.matmul(y_ps[n % NY][:, :], m_slots[i][:, c * P:(c + 1) * P],
                                 x_slots[i][:, :], start=True, stop=True).then_inc(y_mm, 1)

            def head(pair):
                select_x(pair, 0)
                scores(pair)
                select_x(pair, 1)

            with pe.Fori(0, LAST) as g:
                head(g)
                bx(g + 1, 0, 0, C)
                delta(g)
                bx(g + 1, 1, 0, 5)
                select_m(g)
                done = 5
                for n in range(2 * C):
                    update(g, n)
                    if n % 3 == 2 and done < C:
                        bx(g + 1, 1, done, done + 1)
                        done += 1
                bx(g + 1, 1, done, C)
            head(LAST)
            delta(LAST)
            select_m(LAST)
            for n in range(2 * C):
                update(LAST, n)

        @block.scalar
        def _(act):
            act.wait_ge(w_used, WP)
            for j in range(OJ // 2):
                for g in range(PAIRS):
                    nc.scalar.copy(pw[2 * R * j:2 * R * (j + 1), g, :],
                                   p_ps[j][2 * R * g:2 * R * (g + 1), :]).then_inc(pw_act, 1)
            act.wait_ge(ones_set, 1)

            def x_parts(pair, i):
                act.wait_ge(bx_done[i], pair + 1)
                nc.scalar.activation(x_part[i][0][:, :], bx_ps[i][0:R, :], ACT.Copy,
                                     accum_out=x_sum[i][:, :]).then_inc(x1_done[i], 1)
                act.wait_ge(x1_done[i], pair + 1)
                nc.scalar.mul(sum_wide[i][:, :], ones[:, :], x_sum[i][:, :]).then_inc(wide_done[i], 1)
                act.wait_ge(xr_done[i], pair + 1)
                nc.scalar.copy(x_part[i][1][:, :], x_rest[:, :]).then_inc(x2_done[i], 1)

            def x_to_slots(pair, i):
                act.wait_ge(xsel_mm[i], pair + 1)
                nc.scalar.copy(x_slots[i][:, :], sel_ps[i][:, :]).then_inc(x_slots_done[i], 1)

            def exponentials(pair):
                act.wait_ge(dif_done, pair + 1)
                nc.scalar.activation(sexp[:, :, :], sdif[:, :, :], ACT.Exp,
                                     scale=SCORE_SCALE).then_inc(exp_done, 1)

            def m_parts(pair):
                act.wait_ge(mf_done, pair + 1)
                nc.scalar.copy(m_part[0][:, :], m_rest[:, :]).then_inc(m1_done, 1)
                act.wait_ge(mr_done, pair + 1)
                nc.scalar.copy(m_part[1][:, :], m_rest[:, :]).then_inc(m2_done, 1)

            def m_to_slots(pair):
                for n in range(2 * OJ):
                    act.wait_ge(msel_mm, pair * 2 * OJ + n + 1)
                    nc.scalar.copy(m_slots[n // OJ][:, (n % OJ) * S:(n % OJ + 1) * S],
                                   sel_ps[n % 2][:, :]).then_inc(m_slots_done, 1)

            x_parts(0, 0)
            x_parts(0, 1)
            with act.Fori(0, LAST) as g:
                x_to_slots(g, 0)
                x_to_slots(g, 1)
                exponentials(g)
                x_parts(g + 1, 0)
                m_parts(g)
                m_to_slots(g)
                x_parts(g + 1, 1)
            x_to_slots(LAST, 0)
            x_to_slots(LAST, 1)
            exponentials(LAST)
            m_parts(LAST)
            m_to_slots(LAST)

        @block.vector
        def _(dve):
            nc.vector.memset(ones[:, :], 1.0).then_inc(ones_set, 1)
            dve.wait_ge(a_in, 16 * NB)
            for b in range(NB):
                nc.vector.tensor_copy(a_ord[:, :, b * R:(b + 1) * R], a_raw[:, b, :, :]).then_inc(a_ordered, 1)
            dve.wait_ge(w_used, WP)
            nc.vector.tensor_copy(m_rest[:, :], g_ps[:, :]).then_inc(g_copied, 1)
            nc.vector.tensor_copy(wat_sb, wat_ps[:, 0:NB * R]).then_inc(wat_copied, 1)
            for j in range(OJ // 2, OJ):
                for g in range(PAIRS):
                    nc.vector.tensor_copy(pw[2 * R * j:2 * R * (j + 1), g, :],
                                          p_ps[j][2 * R * g:2 * R * (g + 1), :]).then_inc(pw_dve, 1)

            def x_rests(pair, i):
                dve.wait_ge(x1_done[i], pair + 1)
                nc.vector.tensor_tensor(x_rest[:, :], bx_ps[i][0:R, :], x_part[i][0][:, :],
                                        ALU.subtract).then_inc(xr_done[i], 1)
                dve.wait_ge(x2_done[i], pair + 1)
                nc.vector.tensor_tensor(x_part[i][2][:, :], x_rest[:, :], x_part[i][1][:, :],
                                        ALU.subtract).then_inc(x3_done[i], 1)
                dve.wait_ge(x3_done[i], pair + 1)

            def coefficients(pair):
                dve.wait_ge(scores_mm, pair + 1)
                s = m_ps[:, 0:2 * E].rearrange("p (i e) -> p i e", i=2)
                nc.vector.reduce_max(smax[:, :], s, AX.X).then_inc(max_done, 1)
                dve.wait_ge(max_done, pair + 1)
                nc.vector.tensor_tensor(sdif[:, :, :], s, smax[:, :].unsqueeze(2).broadcast_to([P, 2, E]),
                                        ALU.subtract).then_inc(dif_done, 1)
                dve.wait_ge(exp_done, pair + 1)
                nc.vector.reduce_sum(ssum[:, :], sexp[:, :, :], AX.X).then_inc(sum_done, 1)
                dve.wait_ge(sum_done, pair + 1)
                nc.vector.reciprocal(srec[:, :], ssum[:, :]).then_inc(rec_done, 1)
                dve.wait_ge(rec_done, pair + 1)
                nc.vector.tensor_tensor(coef[:, :, :], sexp[:, :, :], srec[:, :].unsqueeze(2).broadcast_to([P, 2, E]),
                                        ALU.mult).then_inc(coef_done, 1)
                dve.wait_ge(coef_done, pair + 1)
                ce = coef[:, :, :].rearrange("p i (k h) -> p k i h", h=2)
                for h in range(2):
                    rows = slice(h * P // 2, (h + 1) * P // 2)
                    g_in = gt[rows, :, bass.ds(pair * (2 * R), 2 * R)].rearrange("p k (i r) -> p k i r", i=2)
                    nc.vector.tensor_tensor(g_scaled[rows, :, :, :], g_in,
                                            ce[rows, :, :, h].unsqueeze(3).broadcast_to([P // 2, KE, 2, R]),
                                            ALU.mult).then_inc(g_scaled_done, 1)

            def m_rests(pair):
                dve.wait_ge(delta_mm, pair + 1)
                nc.vector.tensor_tensor(m_rest[:, :], m_ps[:, :],
                                        pw[:, bass.ds(pair, 1), :].rearrange("p g t -> p (g t)"),
                                        ALU.add).then_inc(mf_done, 1)
                dve.wait_ge(m1_done, pair + 1)
                nc.vector.tensor_tensor(m_rest[:, :], m_rest[:, :], m_part[0][:, :],
                                        ALU.subtract).then_inc(mr_done, 1)
                dve.wait_ge(m2_done, pair + 1)
                nc.vector.tensor_tensor(m_part[2][:, :], m_rest[:, :], m_part[1][:, :],
                                        ALU.subtract).then_inc(m3_done, 1)

            def add_updates(pair):
                for n in range(2 * C):
                    dve.wait_ge(y_mm, pair * 2 * C + n + 1)
                    xc = chunks(pair, n // C, n % C)
                    nc.vector.tensor_tensor(xc, y_ps[n % NY][:, :], xc, ALU.add).then_inc(y_added, 1)

            dve.wait_ge(gt_mm, 1)
            nc.vector.tensor_copy(gt[:, :, :].rearrange("p k m -> p (k m)"), g_ps[:, :]).then_inc(gt_copied, 1)
            dve.wait_ge(ka_mm, 1)
            nc.vector.tensor_copy(ka[:, :, :].rearrange("r b e -> r (b e)"),
                                  wat_ps[0:R, 0:NB * E]).then_inc(ka_copied, 1)
            x_rests(0, 0)
            x_rests(0, 1)
            dve.wait_ge(gt_copied, 1)
            dve.wait_ge(pw_act, 2 * PAIRS)
            dve.wait_ge(pw_dve, 2 * PAIRS)
            with dve.Fori(0, LAST) as g:
                coefficients(g)
                x_rests(g + 1, 0)
                m_rests(g)
                add_updates(g)
                x_rests(g + 1, 1)
            coefficients(LAST)
            m_rests(LAST)
            add_updates(LAST)

        @block.gpsimd
        def _(pool):
            def b_to_place(pair, i):
                nc.gpsimd.tensor_copy(b_cur[i][:, :],
                                      b_all[:, bass.ds(pair * 2 + i, 1), :].rearrange("p b m -> p (b m)")
                                      ).then_inc(b_ready[i], 1)

            pool.wait_ge(b_in, 16 * NB)
            for i in range(2):
                b_to_place(0, i)
            with pool.Fori(1, PAIRS) as g:
                for i in range(2):
                    pool.wait_ge(bx_done[i], g + 0)
                    b_to_place(g, i)


def kernel(**inputs):
    import numpy as np
    import ml_dtypes
    import concourse.bacc as bacc
    from concourse.bass_utils import run_bass_kernel_spmd

    x = np.asarray(inputs["x"])
    ids = np.asarray(inputs["itok_B_3_7"])
    A = np.asarray(inputs["L0_cond_A"])
    B = np.asarray(inputs["L0_cond_B"])
    W = np.asarray(inputs["L0_ffn_W_org"])
    down = np.asarray(inputs["L0_ffn_lora_down"])
    up = np.asarray(inputs["L0_ffn_lora_up"])
    keys = np.asarray(inputs["L0_ffn_lora_keys"])
    Wq = np.asarray(inputs["L0_ffn_Wq"])
    NB, S, D = x.shape
    NA, R = A.shape[0], A.shape[2]
    C = D // P
    E, _, RE = down.shape
    K = Wq.shape[0]

    def by_chunk(t):
        return t.reshape(C, P, -1).transpose(1, 0, 2)

    sel_x = np.zeros((R, 3, P), ml_dtypes.bfloat16)
    sel_m = np.zeros((P, 3, 2, P), ml_dtypes.bfloat16)
    for s, (mp, xp) in enumerate(PRODUCTS):
        for r in range(R):
            sel_x[r, xp, s * R + r] = 1
            for i in range(2):
                sel_m[i * R + r::2 * R, mp, i, s * R + r] = 1

    arrays = {
        "x": x.reshape(NB, S, C, P).transpose(0, 3, 2, 1),
        "ids": ids.reshape(1, NB),
        "a_tab": A.reshape(NA, C, P, R).transpose(0, 2, 1, 3),
        "b_tab": B.reshape(NA, R, C, P).transpose(0, 3, 2, 1),
        "w_cat": np.concatenate([by_chunk(W.T), by_chunk(down.transpose(1, 0, 2).reshape(D, E * RE)),
                                 by_chunk(Wq.T)], axis=2),
        "up": up.reshape(E * RE // P, P, D).transpose(1, 0, 2),
        "keys_t": keys.T,
        "ident": np.eye(P, dtype=np.float32),
        "sel_x": sel_x,
        "sel_m": sel_m,
    }
    nc = bacc.Bacc("TRN2", target_bir_lowering=False, num_devices=1)
    args = {}
    for name in arrays:
        arrays[name] = np.ascontiguousarray(arrays[name])
        args[name] = nc.dram_tensor(f"in_{name}", arrays[name].shape,
                                    mybir.dt.from_np(arrays[name].dtype), kind="ExternalInput").ap()
    out = nc.dram_tensor("out_y", (NB, P, C, S), F32, kind="ExternalOutput").ap()
    lora_ffn(nc, *args.values(), out)
    r = run_bass_kernel_spmd(nc, [{f"in_{n}": a for n, a in arrays.items()}], core_ids=[0])
    y = r.results[0]["out_y"]
    return y.transpose(0, 3, 2, 1).reshape(NB, S, D)
```

```python
import concourse.bass as bass
from concourse import mybir
from contextlib import ExitStack

F32 = mybir.dt.float32
BF16 = mybir.dt.bfloat16
ALU = mybir.AluOpType
ACT = mybir.ActivationFunctionType
AX = mybir.AxisListType

P = 128
TILE = 32
PRODUCTS = ((0, 0), (0, 1), (1, 0), (0, 2), (2, 0), (1, 1), (1, 2), (2, 1))


def lora_ffn(nc, x, ids, a_tab, b_tab, w_cat, up, keys_t, ident, sum_x, less, sel_m, y):
    NB, _, C, S = x.shape
    NA, _, _, R = a_tab.shape
    O = up.shape[2]
    CW = w_cat.shape[2]
    ER = CW - O - P
    KE = ER // P
    K, E = keys_t.shape
    PAIRS = NB // 2
    LAST = PAIRS - 1
    OJ = O // S
    WRING = 6
    XP = 4
    XC = C // XP
    SLOTS = 4
    SCORE_SCALE = 1.0 / (S * float(K) ** 0.5)
    assert len(PRODUCTS) * R == P and 2 * R == TILE and TILE * OJ == P and E == 2 * KE

    ctx = ExitStack()
    with ctx:
        def sb(name, shape, dt):
            return ctx.enter_context(nc.sbuf_tensor(name, shape, dt))

        def pb(name):
            return ctx.enter_context(nc.psum_tensor(name, [P, S], F32))

        def sem(name):
            return ctx.enter_context(nc.semaphore(name))

        xs = sb("xs", [P, SLOTS * C * S], F32)
        up_sb = sb("up_sb", [P, KE, O], F32)
        pw = sb("pw", [P, PAIRS, S], F32)
        gt = sb("gt", [P, KE, NB * R], F32)
        a_ord = sb("a_ord", [P, C, NB * R], F32)
        b_sb = [sb(f"b_sb{i}", [P, C * R], F32) for i in range(2)]
        x_quarters = sb("x_quarters", [P, S], F32)
        x_part1 = sb("x_part1", [P, S], BF16)
        x_left = sb("x_left", [P, S], F32)
        x_part2 = sb("x_part2", [P, S], BF16)
        x_rows = sb("x_rows", [P, SLOTS, S], BF16)
        m_left = sb("m_left", [P, S], F32)
        m_part = [sb(f"m_part{k}", [P, S], BF16) for k in range(3)]
        m_rows = [sb(f"m_rows{i}", [P, O], BF16) for i in range(2)]
        g_scaled = sb("g_scaled", [P, KE, 2, R], F32)
        sumx_sb = sb("sumx_sb", [P, P], F32)
        less_sb = sb("less_sb", [P, 2], F32)
        selm_sb = sb("selm_sb", [P, 3, 2, P], BF16)
        ident_sb = sb("ident_sb", [P, P], F32)
        wat_sb = sb("wat_sb", [P, NB * R], F32)
        keys_sb = sb("keys_sb", [P, E], F32)
        ka = sb("ka", [R, NB, E], F32)
        ones = sb("ones", [R, P], F32)
        x_sum = [sb(f"x_sum{i}", [P, 1], F32) for i in range(2)]
        sum_wide = [sb(f"sum_wide{i}", [R, P], F32) for i in range(2)]
        smax = sb("smax", [P, 2], F32)
        sdif = sb("sdif", [P, 2, E], F32)
        sexp = sb("sexp", [P, 2, E], F32)
        ssum = sb("ssum", [P, 2], F32)
        srec = sb("srec", [P, 2], F32)
        coef = sb("coef", [P, 2, E], F32)

        a_raw = xs[:, C * S:C * S + NB * C * R].rearrange("p (b c r) -> p b c r", b=NB, c=C)
        w_ring = xs[:, 2 * C * S:2 * C * S + WRING * CW].rearrange("p (n m) -> p n m", n=WRING)

        bx_ps = pb("bx_ps")
        x_row_ps = pb("x_row_ps")
        m_ps = pb("m_ps")
        m_row_ps = pb("m_row_ps")
        y_ps = [pb(f"y_ps{i}") for i in range(4)]
        NY = len(y_ps)
        p_ps, g_ps, wat_ps = y_ps, x_row_ps, m_ps

        const_in = sem("const_in")
        a_in = sem("a_in")
        b_in = [sem(f"b_in{i}") for i in range(2)]
        up_in = sem("up_in")
        w_in = [sem(f"w_in{i}") for i in range(WRING)]
        x_in = [[sem(f"x_in{i}_{k}") for k in range(XP)] for i in range(2)]
        stored = [[sem(f"stored{i}_{k}") for k in range(XP)] for i in range(2)]
        ones_set = sem("ones_set")
        bx_cleared = sem("bx_cleared")
        a_ordered = sem("a_ordered")
        w_used = sem("w_used")
        g_copied = sem("g_copied")
        wat_copied = sem("wat_copied")
        pw_act = sem("pw_act")
        pw_dve = sem("pw_dve")
        gt_mm = sem("gt_mm")
        ka_mm = sem("ka_mm")
        gt_copied = sem("gt_copied")
        ka_copied = sem("ka_copied")
        bx_mm = [sem(f"bx_mm{i}") for i in range(2)]
        quarters_done = [sem(f"quarters_done{i}") for i in range(2)]
        x_mm = [sem(f"x_mm{i}") for i in range(2)]
        x1_done = [sem(f"x1_done{i}") for i in range(2)]
        wide_done = [sem(f"wide_done{i}") for i in range(2)]
        xl_done = [sem(f"xl_done{i}") for i in range(2)]
        x2_done = [sem(f"x2_done{i}") for i in range(2)]
        x_rows_done = [sem(f"x_rows_done{i}") for i in range(2)]
        scores_mm = sem("scores_mm")
        max_done = sem("max_done")
        dif_done = sem("dif_done")
        exp_done = sem("exp_done")
        sum_done = sem("sum_done")
        rec_done = sem("rec_done")
        coef_done = sem("coef_done")
        g_scaled_done = sem("g_scaled_done")
        delta_mm = sem("delta_mm")
        m_sum_done = sem("m_sum_done")
        m1_done = sem("m1_done")
        ml_done = sem("ml_done")
        m2_done = sem("m2_done")
        m3_done = sem("m3_done")
        m_rows_mm = sem("m_rows_mm")
        m_rows_done = sem("m_rows_done")
        y_mm = sem("y_mm")
        y_added = sem("y_added")

        block = ctx.enter_context(nc.Block())

        def slot_of(pair, i):
            return (pair % 2) * 2 + i

        def chunks(pair, i, c, n=1):
            return xs[:, bass.ds((slot_of(pair, i) * C + c) * S, n * S)]

        def x_rows_of(pair, i):
            return x_rows[:, bass.ds(slot_of(pair, i), 1), :].rearrange("p s t -> p (s t)")

        @block.sync
        def _(sp):
            def in_dram(t, b, k):
                return t[b, :, k * XC:(k + 1) * XC, :].rearrange("p c t -> p (c t)")

            def load_w(n):
                if n >= WRING:
                    sp.wait_ge(w_used, n - WRING + 1)
                sp.dma_start(w_ring[:, n % WRING, :], w_cat[:, n, :]).then_inc(w_in[n % WRING], 16)

            def of_adapter(table, b):
                return table[bass.ds(adapter[b], 1), :, :, :].rearrange("a p c r -> (a p) (c r)")

            def load_b(b):
                if b >= 2:
                    sp.wait_ge(bx_mm[b % 2], b // 2)
                sp.dma_start(b_sb[b % 2][:, :], of_adapter(b_tab, b)).then_inc(b_in[b % 2], 16)

            def load_x(b, k):
                pair, i = b // 2, b % 2
                if b >= 2:
                    sp.wait_ge(x_in[i][k], 16 * pair)
                if b >= SLOTS:
                    sp.wait_ge(stored[i][k], 16 * (pair - 1))
                sp.dma_start(chunks(pair, i, k * XC, XC), in_dram(x, b, k)).then_inc(x_in[i][k], 16)

            def store(b, k):
                pair, i = b // 2, b % 2
                sp.wait_ge(y_added, b * C + (k + 1) * XC)
                sp.dma_start(in_dram(y, b, k), chunks(pair, i, k * XC, XC)).then_inc(stored[i][k], 16)

            load_w(0)
            _, adapter = nc.values_load_multi_w_load_instructions(
                ids[0:1, 0:NB], engines=[mybir.EngineType.SP], min_val=0, max_val=NA - 1)
            for b in range(NB):
                sp.dma_start(a_raw[:, b, :, :].rearrange("p c r -> p (c r)"),
                             of_adapter(a_tab, b)).then_inc(a_in, 16)
            for n in range(1, WRING):
                load_w(n)
            load_b(0)
            load_b(1)
            for dst, src in ((ident_sb[:, :], ident), (keys_sb[:, :], keys_t), (sumx_sb[:, :], sum_x),
                             (less_sb[:, :], less), (selm_sb[:, :, :, :], sel_m)):
                sp.dma_start(dst, src).then_inc(const_in, 16)
            for n in range(WRING, C):
                load_w(n)
            for k in range(XP):
                load_x(0, k)
            sp.wait_ge(a_ordered, XP)
            for k in range(XP):
                load_x(1, k)
            sp.dma_start(up_sb[:, :, :], up).then_inc(up_in, 16)
            sp.wait_ge(w_used, C)
            for b in (2, 3):
                load_b(b)
                for k in range(XP):
                    load_x(b, k)
            for b in range(NB):
                for k in range(XP):
                    store(b, k)
                    if b + SLOTS < NB:
                        if k == 1:
                            load_b(b + SLOTS)
                        if k > 0:
                            load_x(b + SLOTS, k - 1)
                if b + SLOTS < NB:
                    load_x(b + SLOTS, XP - 1)
            for i in range(2):
                for k in range(XP):
                    sp.wait_ge(stored[i][k], 16 * PAIRS)

        @block.tensor
        def _(pe):
            for c in range(C):
                pe.wait_ge(w_in[c % WRING], 16 * (c // WRING + 1))
                if c % XC == 0:
                    pe.wait_ge(a_ordered, c // XC + 1)
                w = w_ring[:, c % WRING, :]
                on = dict(start=(c == 0), stop=(c == C - 1))
                for j in range(OJ):
                    nc.tensor.matmul(p_ps[j][:, :], a_ord[:, c, :], w[:, j * S:(j + 1) * S], **on)
                nc.tensor.matmul(g_ps[:, :], a_ord[:, c, :], w[:, O:O + ER], **on)
                nc.tensor.matmul(wat_ps[:, 0:NB * R], w[:, O + ER:CW], a_ord[:, c, :],
                                 **on).then_inc(w_used, 1)

            def bx(pair, i, q):
                if q == 0:
                    pe.wait_ge(b_in[i], pair * 16 + 16)
                    if i == 1:
                        pe.wait_ge(quarters_done[0], pair + 1)
                    elif pair > 0:
                        pe.wait_ge(quarters_done[1], pair)
                pe.wait_ge(x_in[i][q], pair * 16 + 16)
                for c in range(q * XC, (q + 1) * XC):
                    at = c % 4 * TILE
                    mm = nc.tensor.matmul(bx_ps[at:at + R, :], b_sb[i][:, c * R:(c + 1) * R],
                                          chunks(pair, i, c), start=(c < 4), stop=(c >= C - 4))
                if q == XP - 1:
                    mm.then_inc(bx_mm[i], 1)

            def add_quarters(pair, i):
                pe.wait_ge(quarters_done[i], pair + 1)
                if i == 1:
                    pe.wait_ge(xl_done[0], pair + 1)
                elif pair > 0:
                    pe.wait_ge(xl_done[1], pair)
                nc.tensor.matmul(x_row_ps[:, :], sumx_sb[:, :], x_quarters[:, :],
                                 start=True, stop=True).then_inc(x_mm[i], 1)

            def scores(pair):
                for i in range(2):
                    pe.wait_ge(wide_done[i], pair + 1)
                    mm = nc.tensor.matmul(m_ps[:, i * E:(i + 1) * E], sum_wide[i][:, :],
                                          ka[:, bass.ds(pair * 2 + i, 1), :].rearrange("r b e -> r (b e)"),
                                          start=True, stop=True)
                mm.then_inc(scores_mm, 1)

            def delta(pair):
                pe.wait_ge(g_scaled_done, pair * 2 + 2)
                for k in range(KE):
                    for j in range(OJ):
                        mm = nc.tensor.matmul(m_ps[TILE * j:TILE * (j + 1), :],
                                              g_scaled[:, k, :, :].rearrange("p i r -> p (i r)"),
                                              up_sb[:, k, j * S:(j + 1) * S],
                                              start=(k == 0), stop=(k == KE - 1))
                mm.then_inc(delta_mm, 1)

            def m_to_rows(pair, n):
                if n == 0:
                    pe.wait_ge(m3_done, pair + 1)
                if pair + n > 0:
                    pe.wait_ge(m_rows_done, pair * 2 * OJ + n)
                quad = slice(TILE * (n % OJ), TILE * (n % OJ + 1))
                for k in range(3):
                    mm = nc.tensor.matmul(m_row_ps[:, :], selm_sb[quad, k, n // OJ, :],
                                          m_part[k][quad, :], start=(k == 0), stop=(k == 2))
                mm.then_inc(m_rows_mm, 1)

            def updates(pair, first, end):
                for n in range(first, end):
                    i, c = n // C, n % C
                    if c % 4 == 0:
                        pe.wait_ge(m_rows_done, pair * 2 * OJ + i * OJ + c // 4 + 1)
                    if n == 0 and pair > 0:
                        pe.wait_ge(y_added, pair * 2 * C)
                    if n >= NY:
                        pe.wait_ge(y_added, pair * 2 * C + n - NY + 1)
                    nc.tensor.matmul(y_ps[n % NY][:, :], m_rows[i][:, c * P:(c + 1) * P],
                                     x_rows_of(pair, i), start=True, stop=True).then_inc(y_mm, 1)

            pe.wait_ge(bx_cleared, 1)
            for q in range(XP):
                bx(0, 0, q)
            pe.wait_ge(const_in, 16 * 5)
            pe.wait_ge(g_copied, 1)
            for k in range(KE):
                mm = nc.tensor.transpose(g_ps[:, k * P:(k + 1) * P], m_left[:, k * P:(k + 1) * P],
                                         ident_sb[:, :])
            mm.then_inc(gt_mm, 1)
            pe.wait_ge(wat_copied, 1)
            for b in range(NB):
                mm = nc.tensor.matmul(wat_ps[0:R, b * E:(b + 1) * E], wat_sb[:, b * R:(b + 1) * R],
                                      keys_sb[:, :], start=True, stop=True)
            mm.then_inc(ka_mm, 1)
            pe.wait_ge(pw_act, 2 * PAIRS)
            pe.wait_ge(pw_dve, 2 * PAIRS)
            pe.wait_ge(gt_copied, 1)
            pe.wait_ge(ka_copied, 1)
            add_quarters(0, 0)
            for q in range(XP):
                bx(0, 1, q)
            add_quarters(0, 1)
            scores(0)
            pe.wait_ge(up_in, 16)
            delta(0)
            for g in range(LAST):
                m_to_rows(g, 0)
                for i in range(2):
                    u, m = i * 12, i * 3
                    m_to_rows(g, m + 1)
                    updates(g, u, u + 2)
                    bx(g + 1, i, 0)
                    updates(g, u + 2, u + 4)
                    bx(g + 1, i, 1)
                    m_to_rows(g, m + 2)
                    updates(g, u + 4, u + 6)
                    bx(g + 1, i, 2)
                    updates(g, u + 6, u + 8)
                    bx(g + 1, i, 3)
                    m_to_rows(g, m + 3)
                    updates(g, u + 8, u + 10)
                    add_quarters(g + 1, i)
                    updates(g, u + 10, u + 12)
                m_to_rows(g, 7)
                updates(g, 24, 25)
                scores(g + 1)
                updates(g, 25, 28)
                delta(g + 1)
                updates(g, 28, 32)
            m_to_rows(LAST, 0)
            for n in range(1, 2 * OJ):
                m_to_rows(LAST, n)
                updates(LAST, (n - 1) * XC, n * XC)
            updates(LAST, 2 * C - XC, 2 * C)

        @block.scalar
        def _(act):
            def quarters(pair, i):
                act.wait_ge(bx_mm[i], pair + 1)
                if i == 1:
                    act.wait_ge(x_mm[0], pair + 1)
                elif not (isinstance(pair, int) and pair == 0):
                    act.wait_ge(x_mm[1], pair + 0)
                nc.scalar.copy(x_quarters[:, :], bx_ps[:, :]).then_inc(quarters_done[i], 1)

            def x_parts_1(pair, i):
                act.wait_ge(x_mm[i], pair + 1)
                if i == 1:
                    act.wait_ge(x_rows_done[0], pair + 1)
                elif not (isinstance(pair, int) and pair == 0):
                    act.wait_ge(x_rows_done[1], pair + 0)
                nc.scalar.activation(x_part1[:, :], x_row_ps[:, :], ACT.Copy,
                                     accum_out=x_sum[i][:, :]).then_inc(x1_done[i], 1)
                act.wait_ge(x1_done[i], pair + 1)
                nc.scalar.mul(sum_wide[i][:, :], ones[:, :], x_sum[i][0:R, :]).then_inc(wide_done[i], 1)

            def x_parts_2(pair, i):
                act.wait_ge(xl_done[i], pair + 1)
                nc.scalar.copy(x_part2[:, :], x_left[:, :]).then_inc(x2_done[i], 1)

            def exponentials(pair):
                act.wait_ge(dif_done, pair + 1)
                nc.scalar.activation(sexp[:, :, :], sdif[:, :, :], ACT.Exp,
                                     scale=SCORE_SCALE).then_inc(exp_done, 1)

            def m_parts(pair):
                act.wait_ge(m_sum_done, pair + 1)
                nc.scalar.copy(m_part[0][:, :], m_left[:, :]).then_inc(m1_done, 1)
                act.wait_ge(ml_done, pair + 1)
                nc.scalar.copy(m_part[1][:, :], m_left[:, :]).then_inc(m2_done, 1)

            def m_from_rows(pair, first, end):
                for n in range(first, end):
                    act.wait_ge(m_rows_mm, pair * 2 * OJ + n + 1)
                    nc.scalar.copy(m_rows[n // OJ][:, n % OJ * S:(n % OJ + 1) * S],
                                   m_row_ps[:, :]).then_inc(m_rows_done, 1)

            act.wait_ge(w_used, C)
            for j in range(OJ // 2):
                for g in range(PAIRS):
                    nc.scalar.copy(pw[TILE * j:TILE * (j + 1), g, :],
                                   p_ps[j][TILE * g:TILE * (g + 1), :]).then_inc(pw_act, 1)
            act.wait_ge(ones_set, 1)
            for i in range(2):
                quarters(0, i)
                x_parts_1(0, i)
                x_parts_2(0, i)
            exponentials(0)
            m_parts(0)
            with act.Fori(0, LAST) as g:
                m_from_rows(g, 0, 3)
                quarters(g + 1, 0)
                m_from_rows(g, 3, 4)
                x_parts_1(g + 1, 0)
                m_from_rows(g, 4, 5)
                x_parts_2(g + 1, 0)
                m_from_rows(g, 5, 6)
                quarters(g + 1, 1)
                m_from_rows(g, 6, 7)
                x_parts_1(g + 1, 1)
                m_from_rows(g, 7, 8)
                exponentials(g + 1)
                x_parts_2(g + 1, 1)
                m_parts(g + 1)
            m_from_rows(LAST, 0, 2 * OJ)

        @block.vector
        def _(dve):
            def x_less_part1(pair, i):
                dve.wait_ge(x1_done[i], pair + 1)
                nc.vector.scalar_tensor_tensor(x_left[:, :], x_part1[:, :], less_sb[:, 0:1], x_row_ps[:, :],
                                               ALU.mult, ALU.add).then_inc(xl_done[i], 1)

            def x_less_part2(pair, i):
                dve.wait_ge(x2_done[i], pair + 1)
                nc.vector.scalar_tensor_tensor(x_rows_of(pair, i), x_part2[:, :], less_sb[:, 1:2], x_left[:, :],
                                               ALU.mult, ALU.add).then_inc(x_rows_done[i], 1)

            def score_differences(pair):
                dve.wait_ge(scores_mm, pair + 1)
                s = m_ps[:, 0:2 * E].rearrange("p (i e) -> p i e", i=2)
                nc.vector.reduce_max(smax[:, :], s, AX.X).then_inc(max_done, 1)
                dve.wait_ge(max_done, pair + 1)
                nc.vector.tensor_tensor(sdif[:, :, :], s, smax[:, :].unsqueeze(2).broadcast_to([P, 2, E]),
                                        ALU.subtract).then_inc(dif_done, 1)

            def coefficients(pair):
                dve.wait_ge(exp_done, pair + 1)
                nc.vector.reduce_sum(ssum[:, :], sexp[:, :, :], AX.X).then_inc(sum_done, 1)
                dve.wait_ge(sum_done, pair + 1)
                nc.vector.reciprocal(srec[:, :], ssum[:, :]).then_inc(rec_done, 1)
                dve.wait_ge(rec_done, pair + 1)
                nc.vector.tensor_tensor(coef[:, :, :], sexp[:, :, :],
                                        srec[:, :].unsqueeze(2).broadcast_to([P, 2, E]),
                                        ALU.mult).then_inc(coef_done, 1)
                dve.wait_ge(coef_done, pair + 1)
                ce = coef[:, :, :].rearrange("p i (k h) -> p k i h", h=2)
                for h in range(2):
                    half = slice(h * P // 2, (h + 1) * P // 2)
                    g_in = gt[half, :, bass.ds(pair * TILE, TILE)].rearrange("p k (i r) -> p k i r", i=2)
                    nc.vector.tensor_tensor(g_scaled[half, :, :, :], g_in,
                                            ce[half, :, :, h].unsqueeze(3).broadcast_to([P // 2, KE, 2, R]),
                                            ALU.mult).then_inc(g_scaled_done, 1)

            def m_sum(pair):
                dve.wait_ge(delta_mm, pair + 1)
                nc.vector.tensor_tensor(m_left[:, :], m_ps[:, :],
                                        pw[:, bass.ds(pair, 1), :].rearrange("p g t -> p (g t)"),
                                        ALU.add).then_inc(m_sum_done, 1)

            def m_less_part1(pair):
                dve.wait_ge(m1_done, pair + 1)
                nc.vector.tensor_tensor(m_left[:, :], m_left[:, :], m_part[0][:, :],
                                        ALU.subtract).then_inc(ml_done, 1)

            def m_part3(pair):
                dve.wait_ge(m2_done, pair + 1)
                nc.vector.tensor_tensor(m_part[2][:, :], m_left[:, :], m_part[1][:, :],
                                        ALU.subtract).then_inc(m3_done, 1)

            def add_updates(pair, first, end):
                for n in range(first, end):
                    dve.wait_ge(y_mm, pair * 2 * C + n + 1)
                    xc = chunks(pair, n // C, n % C)
                    nc.vector.tensor_tensor(xc, y_ps[n % NY][:, :], xc, ALU.add).then_inc(y_added, 1)

            nc.vector.memset(ones[:, :], 1.0).then_inc(ones_set, 1)
            nc.vector.memset(bx_ps[:, :], 0.0).then_inc(bx_cleared, 1)
            dve.wait_ge(a_in, 16 * NB)
            for k in range(XP):
                cs = slice(k * XC, (k + 1) * XC)
                nc.vector.tensor_copy(a_ord[:, cs, :].rearrange("p c (b r) -> p c b r", b=NB),
                                      a_raw[:, :, cs, :].rearrange("p b c r -> p c b r")).then_inc(a_ordered, 1)
            dve.wait_ge(w_used, C)
            nc.vector.tensor_copy(m_left[:, :], g_ps[:, :]).then_inc(g_copied, 1)
            nc.vector.tensor_copy(wat_sb[:, :], wat_ps[:, 0:NB * R]).then_inc(wat_copied, 1)
            for j in range(OJ // 2, OJ):
                for g in range(PAIRS):
                    nc.vector.tensor_copy(pw[TILE * j:TILE * (j + 1), g, :],
                                          p_ps[j][TILE * g:TILE * (g + 1), :]).then_inc(pw_dve, 1)
            dve.wait_ge(gt_mm, 1)
            nc.vector.tensor_copy(gt[:, :, :].rearrange("p k m -> p (k m)"), g_ps[:, :]).then_inc(gt_copied, 1)
            dve.wait_ge(ka_mm, 1)
            nc.vector.tensor_copy(ka[:, :, :].rearrange("r b e -> r (b e)"),
                                  wat_ps[0:R, 0:NB * E]).then_inc(ka_copied, 1)
            dve.wait_ge(const_in, 16 * 5)
            for i in range(2):
                x_less_part1(0, i)
                x_less_part2(0, i)
            dve.wait_ge(gt_copied, 1)
            score_differences(0)
            coefficients(0)
            dve.wait_ge(pw_act, 2 * PAIRS)
            dve.wait_ge(pw_dve, 2 * PAIRS)
            m_sum(0)
            m_less_part1(0)
            m_part3(0)
            with dve.Fori(0, LAST) as g:
                add_updates(g, 0, 9)
                x_less_part1(g + 1, 0)
                add_updates(g, 9, 12)
                x_less_part2(g + 1, 0)
                add_updates(g, 12, 21)
                x_less_part1(g + 1, 1)
                add_updates(g, 21, 23)
                score_differences(g + 1)
                add_updates(g, 23, 24)
                coefficients(g + 1)
                add_updates(g, 24, 25)
                x_less_part2(g + 1, 1)
                add_updates(g, 25, 28)
                m_sum(g + 1)
                add_updates(g, 28, 29)
                m_less_part1(g + 1)
                add_updates(g, 29, 30)
                m_part3(g + 1)
                add_updates(g, 30, 32)
            add_updates(LAST, 0, 2 * C)


def kernel(**inputs):
    import numpy as np
    import ml_dtypes
    import concourse.bacc as bacc
    from concourse.bass_utils import run_bass_kernel_spmd

    x = np.asarray(inputs["x"])
    ids = np.asarray(inputs["itok_B_3_7"])
    A = np.asarray(inputs["L0_cond_A"])
    B = np.asarray(inputs["L0_cond_B"])
    W = np.asarray(inputs["L0_ffn_W_org"])
    down = np.asarray(inputs["L0_ffn_lora_down"])
    up = np.asarray(inputs["L0_ffn_lora_up"])
    keys = np.asarray(inputs["L0_ffn_lora_keys"])
    Wq = np.asarray(inputs["L0_ffn_Wq"])
    NB, S, D = x.shape
    NA, R = A.shape[0], A.shape[2]
    C = D // P
    E, _, RE = down.shape

    def by_chunk(t):
        return t.reshape(C, P, -1).transpose(1, 0, 2)

    sum_x = np.zeros((P, P), np.float32)
    less = np.zeros((P, 2), np.float32)
    sel_m = np.zeros((P, 3, 2, P), ml_dtypes.bfloat16)
    for s, (mp, xp) in enumerate(PRODUCTS):
        for r in range(R):
            row = s * R + r
            sum_x[r::TILE, row] = 1
            less[row, 0] = -1 if xp > 0 else 0
            less[row, 1] = -1 if xp > 1 else 0
            for i in range(2):
                sel_m[i * R + r::TILE, mp, i, row] = 1

    arrays = {
        "x": x.reshape(NB, S, C, P).transpose(0, 3, 2, 1),
        "ids": ids.reshape(1, NB),
        "a_tab": A.reshape(NA, C, P, R).transpose(0, 2, 1, 3),
        "b_tab": B.reshape(NA, R, C, P).transpose(0, 3, 2, 1),
        "w_cat": np.concatenate([by_chunk(W.T), by_chunk(down.transpose(1, 0, 2).reshape(D, E * RE)),
                                 by_chunk(Wq.T)], axis=2),
        "up": up.reshape(E * RE // P, P, D).transpose(1, 0, 2),
        "keys_t": keys.T,
        "ident": np.eye(P, dtype=np.float32),
        "sum_x": sum_x,
        "less": less,
        "sel_m": sel_m,
    }
    nc = bacc.Bacc("TRN2", target_bir_lowering=False, num_devices=1, dynamic_dma_scratch_size=1024)
    args = {}
    for name in arrays:
        arrays[name] = np.ascontiguousarray(arrays[name])
        args[name] = nc.dram_tensor(f"in_{name}", arrays[name].shape,
                                    mybir.dt.from_np(arrays[name].dtype), kind="ExternalInput").ap()
    out = nc.dram_tensor("out_y", (NB, P, C, S), F32, kind="ExternalOutput").ap()
    lora_ffn(nc, *args.values(), out)
    r = run_bass_kernel_spmd(nc, [{f"in_{n}": a for n, a in arrays.items()}], core_ids=[0])
    y = r.results[0]["out_y"]
    return y.transpose(0, 3, 2, 1).reshape(NB, S, D)
```

```python
import concourse.bass as bass
from concourse import mybir
from contextlib import ExitStack

F32 = mybir.dt.float32
BF16 = mybir.dt.bfloat16
ALU = mybir.AluOpType
ACT = mybir.ActivationFunctionType
AX = mybir.AxisListType

P = 128
TILE = 32
PRODUCTS = ((0, 0), (0, 1), (1, 0), (0, 2), (2, 0), (1, 1), (1, 2), (2, 1))


def lora_ffn(nc, x, ids, a_tab, b_tab, w_cat, up, consts, sel_m, y):
    NB, XP, _, XC, S = x.shape
    C = XP * XC
    NA, _, _, R = a_tab.shape
    O = up.shape[2]
    CW = w_cat.shape[2]
    ER = CW - O - P
    KE = ER // P
    K = P
    E = consts.shape[1] - 2 * P - 2
    PAIRS = NB // 2
    LAST = NB - 1
    OJ = O // S
    WRING = 6
    SLOTS = 4
    LAG = 1
    SCORE_SCALE = 1.0 / (S * float(K) ** 0.5)
    assert len(PRODUCTS) * R == P and 2 * R == TILE and TILE * OJ == P and E == 2 * KE

    ctx = ExitStack()
    with ctx:
        def sb(name, shape, dt):
            return ctx.enter_context(nc.sbuf_tensor(name, shape, dt))

        def pb(name):
            return ctx.enter_context(nc.psum_tensor(name, [P, S], F32))

        def sem(name):
            return ctx.enter_context(nc.semaphore(name))

        xs = sb("xs", [P, SLOTS * C * S], F32)
        up_sb = sb("up_sb", [P, KE, O], F32)
        pw = sb("pw", [P, PAIRS, S], F32)
        gt = sb("gt", [P, KE, NB * R], F32)
        a_ord = sb("a_ord", [P, C, NB * R], F32)
        b_sb = [sb(f"b_sb{i}", [P, C * R], F32) for i in range(SLOTS)]
        x_quarters = sb("x_quarters", [P, S], F32)
        x_part1 = sb("x_part1", [P, S], BF16)
        x_left = sb("x_left", [P, S], F32)
        x_part2 = sb("x_part2", [P, S], BF16)
        x_rows = sb("x_rows", [P, SLOTS, S], BF16)
        m_left = sb("m_left", [P, S], F32)
        m_part = [sb(f"m_part{k}", [P, S], BF16) for k in range(3)]
        m_rows = sb("m_rows", [P, 2, O], BF16)
        g_scaled = sb("g_scaled", [P, KE, 2 * R], F32)
        consts_sb = sb("consts_sb", [P, 2 * P + 2 + E], F32)
        ident_sb = consts_sb[:, 0:P]
        sumx_sb = consts_sb[:, P:2 * P]
        less_sb = consts_sb[:, 2 * P:2 * P + 2]
        keys_sb = consts_sb[:, 2 * P + 2:2 * P + 2 + E]
        selm_sb = sb("selm_sb", [P, 3, 2, P], BF16)
        wat_sb = sb("wat_sb", [P, NB * R], F32)
        ka = sb("ka", [R, NB, E], F32)
        ones = sb("ones", [R, P], F32)
        x_sum = sb("x_sum", [P, 1], F32)
        sum_wide = sb("sum_wide", [R, P], F32)
        smax = sb("smax", [P, 1], F32)
        sdif = sb("sdif", [P, E], F32)
        sexp = sb("sexp", [P, E], F32)
        ssum = sb("ssum", [P, 1], F32)
        srec = sb("srec", [P, 1], F32)
        coef = sb("coef", [P, E], F32)

        a_raw = xs[:, C * S:C * S + NB * C * R].rearrange("p (b c r) -> p b c r", b=NB, c=C)
        w_ring = xs[:, 2 * C * S:2 * C * S + WRING * CW].rearrange("p (n m) -> p n m", n=WRING)

        bx_ps = pb("bx_ps")
        x_row_ps = pb("x_row_ps")
        m_ps = pb("m_ps")
        m_row_ps = pb("m_row_ps")
        y_ps = [pb(f"y_ps{i}") for i in range(4)]
        NY = len(y_ps)
        p_ps, g_ps, wat_ps = y_ps, m_row_ps, m_ps

        const_in = sem("const_in")
        a_in = sem("a_in")
        b_in = [sem(f"b_in{i}") for i in range(SLOTS)]
        up_in = sem("up_in")
        w_in = [sem(f"w_in{i}") for i in range(WRING)]
        x_in = [[sem(f"x_in{i}_{k}") for k in range(XP)] for i in range(SLOTS)]
        stored = [[sem(f"stored{i}_{k}") for k in range(XP)] for i in range(SLOTS)]
        ones_set = sem("ones_set")
        bx_cleared = sem("bx_cleared")
        g_cleared = sem("g_cleared")
        a_ordered = sem("a_ordered")
        w_used = sem("w_used")
        g_copied = sem("g_copied")
        wat_copied = sem("wat_copied")
        pw_act = sem("pw_act")
        pw_dve = sem("pw_dve")
        gt_mm = sem("gt_mm")
        ka_mm = sem("ka_mm")
        gt_copied = sem("gt_copied")
        ka_copied = sem("ka_copied")
        bx_mm = sem("bx_mm")
        quarters_done = sem("quarters_done")
        x_mm = sem("x_mm")
        x1_done = sem("x1_done")
        wide_done = sem("wide_done")
        xl_done = sem("xl_done")
        x2_done = sem("x2_done")
        x_rows_done = sem("x_rows_done")
        scores_mm = sem("scores_mm")
        max_done = sem("max_done")
        dif_done = sem("dif_done")
        exp_done = sem("exp_done")
        sum_done = sem("sum_done")
        rec_done = sem("rec_done")
        coef_done = sem("coef_done")
        g_scaled_done = sem("g_scaled_done")
        delta_mm = sem("delta_mm")
        m_sum_done = sem("m_sum_done")
        m1_done = sem("m1_done")
        ml_done = sem("ml_done")
        m2_done = sem("m2_done")
        m3_done = sem("m3_done")
        m_rows_mm = sem("m_rows_mm")
        m_rows_done = sem("m_rows_done")
        y_mm = sem("y_mm")
        y_added = sem("y_added")

        block = ctx.enter_context(nc.Block())

        def chunks(b, c, n=1):
            return xs[:, bass.ds((b % SLOTS * C + c) * S, n * S)]

        def x_rows_of(b):
            return x_rows[:, bass.ds(b % SLOTS, 1), :].rearrange("p s t -> p (s t)")

        @block.sync
        def _(sp):
            def in_dram(t, b, k):
                return t[b, k, :, :, :].rearrange("p c t -> p (c t)")

            def load_w(n):
                if n >= WRING:
                    sp.wait_ge(w_used, n - WRING + 1)
                sp.dma_start(w_ring[:, n % WRING, :], w_cat[n, :, :]).then_inc(w_in[n % WRING], 16)

            def of_adapter(table, b):
                return table[bass.ds(adapter[b], 1), :, :, :].rearrange("a p c r -> (a p) (c r)")

            def load_b(b):
                if b >= SLOTS:
                    sp.wait_ge(bx_mm, b - SLOTS + 1)
                sp.dma_start(b_sb[b % SLOTS][:, :], of_adapter(b_tab, b)).then_inc(b_in[b % SLOTS], 16)

            def load_x(b, k):
                if b >= SLOTS:
                    sp.wait_ge(stored[b % SLOTS][k], 16 * (b // SLOTS))
                sp.dma_start(chunks(b, k * XC, XC), in_dram(x, b, k)).then_inc(x_in[b % SLOTS][k], 16)

            def store(b, k):
                sp.wait_ge(y_added, b * C + (k + 1) * XC)
                sp.dma_start(in_dram(y, b, k), chunks(b, k * XC, XC)).then_inc(stored[b % SLOTS][k], 16)

            load_w(0)
            _, adapter = nc.values_load_multi_w_load_instructions(
                ids[0:1, 0:NB], engines=[mybir.EngineType.SP], min_val=0, max_val=NA - 1)
            for b in range(NB):
                sp.dma_start(a_raw[:, b, :, :].rearrange("p c r -> p (c r)"),
                             of_adapter(a_tab, b)).then_inc(a_in, 16)
            for n in range(1, WRING):
                load_w(n)
            for b in range(SLOTS):
                load_b(b)
            sp.dma_start(consts_sb[:, :], consts).then_inc(const_in, 16)
            sp.dma_start(selm_sb[:, :, :, :], sel_m).then_inc(const_in, 16)
            for n in range(WRING, C):
                load_w(n)
            for k in range(XP):
                load_x(0, k)
            sp.dma_start(up_sb[:, :, :], up).then_inc(up_in, 16)
            sp.wait_ge(a_ordered, XP)
            for k in range(XP):
                load_x(1, k)
            sp.wait_ge(w_used, C)
            for b in (2, 3):
                for k in range(XP):
                    load_x(b, k)
            for n in range(NB * XP + LAG):
                if n < NB * XP:
                    store(n // XP, n % XP)
                b, k = (n - LAG) // XP + SLOTS, (n - LAG) % XP
                if n >= LAG and b < NB:
                    if k == 0:
                        load_b(b)
                    load_x(b, k)
            for i in range(SLOTS):
                for k in range(XP):
                    sp.wait_ge(stored[i][k], 16 * (NB // SLOTS))

        @block.tensor
        def _(pe):
            def bx(b, q):
                if q == 0:
                    pe.wait_ge(b_in[b % SLOTS], (b // SLOTS + 1) * 16)
                    if b > 0:
                        pe.wait_ge(quarters_done, b)
                pe.wait_ge(x_in[b % SLOTS][q], (b // SLOTS + 1) * 16)
                for c in range(q * XC, (q + 1) * XC):
                    at = c % 4 * TILE
                    mm = nc.tensor.matmul(bx_ps[at:at + R, :], b_sb[b % SLOTS][:, c * R:(c + 1) * R],
                                          chunks(b, c), start=(c < 4), stop=(c >= C - 4))
                if q == XP - 1:
                    mm.then_inc(bx_mm, 1)

            def add_quarters(b):
                pe.wait_ge(quarters_done, b + 1)
                if b > 0:
                    pe.wait_ge(xl_done, b)
                nc.tensor.matmul(x_row_ps[:, :], sumx_sb, x_quarters[:, :],
                                 start=True, stop=True).then_inc(x_mm, 1)

            def scores(b):
                pe.wait_ge(wide_done, b + 1)
                nc.tensor.matmul(m_ps[:, 0:E], sum_wide[:, :], ka[:, b, :],
                                 start=True, stop=True).then_inc(scores_mm, 1)

            def delta(b, k):
                if k == 0:
                    pe.wait_ge(g_scaled_done, b * 2 + 2)
                for j in range(OJ):
                    mm = nc.tensor.matmul(m_ps[TILE * j:TILE * (j + 1), :], g_scaled[:, k, :],
                                          up_sb[:, k, j * S:(j + 1) * S],
                                          start=(k == 0), stop=(k == KE - 1))
                if k == KE - 1:
                    mm.then_inc(delta_mm, 1)

            def m_to_rows(b, j):
                if j == 0:
                    pe.wait_ge(m3_done, b + 1)
                if b + j > 0:
                    pe.wait_ge(m_rows_done, b * OJ + j)
                quad = slice(TILE * j, TILE * (j + 1))
                for k in range(3):
                    mm = nc.tensor.matmul(m_row_ps[:, :], selm_sb[quad, k, b % 2, :],
                                          m_part[k][quad, :], start=(k == 0), stop=(k == 2))
                mm.then_inc(m_rows_mm, 1)

            def updates(b, first, end):
                for c in range(first, end):
                    if c % 4 == 0:
                        pe.wait_ge(m_rows_done, b * OJ + c // 4 + 1)
                    if b * C + c >= NY:
                        pe.wait_ge(y_added, b * C + c - NY + 1)
                    nc.tensor.matmul(y_ps[c % NY][:, :], m_rows[:, b % 2, c * P:(c + 1) * P],
                                     x_rows_of(b), start=True, stop=True).then_inc(y_mm, 1)

            for c in range(C):
                if c == C - 1:
                    pe.wait_ge(bx_cleared, 1)
                    for q in range(XP):
                        bx(0, q)
                pe.wait_ge(w_in[c % WRING], 16 * (c // WRING + 1))
                if c % XC == 0:
                    pe.wait_ge(a_ordered, c // XC + 1)
                w = w_ring[:, c % WRING, :]
                on = dict(start=(c == 0), stop=(c == C - 1))
                for j in range(OJ):
                    nc.tensor.matmul(p_ps[j][:, :], a_ord[:, c, :], w[:, j * S:(j + 1) * S], **on)
                nc.tensor.matmul(g_ps[:, :], a_ord[:, c, :], w[:, O:O + ER], **on)
                nc.tensor.matmul(wat_ps[:, 0:NB * R], w[:, O + ER:CW], a_ord[:, c, :],
                                 **on).then_inc(w_used, 1)
            pe.wait_ge(const_in, 16 * 2)
            add_quarters(0)
            pe.wait_ge(wat_copied, 1)
            for b in range(NB):
                mm = nc.tensor.matmul(wat_ps[0:R, b * E:(b + 1) * E], wat_sb[:, b * R:(b + 1) * R],
                                      keys_sb, start=True, stop=True)
            mm.then_inc(ka_mm, 1)
            pe.wait_ge(g_copied, 1)
            for k in range(KE):
                mm = nc.tensor.transpose(g_ps[:, k * P:(k + 1) * P], m_left[:, k * P:(k + 1) * P], ident_sb)
            mm.then_inc(gt_mm, 1)
            pe.wait_ge(ka_copied, 1)
            scores(0)
            pe.wait_ge(g_cleared, 1)
            pe.wait_ge(up_in, 16)
            for k in range(KE):
                delta(0, k)
            for q in range(XP):
                bx(1, q)
            add_quarters(1)
            m_to_rows(0, 0)
            scores(1)
            m_to_rows(0, 1)
            m_to_rows(0, 2)
            for b in range(LAST):
                for k in range(KE):
                    delta(b + 1, k)
                    updates(b, k, k + 1)
                    if k == 0:
                        m_to_rows(b, 3)
                if b + 2 < NB:
                    for q in range(XP):
                        bx(b + 2, q)
                        updates(b, 4 + q, 5 + q)
                    updates(b, 8, 9)
                    add_quarters(b + 2)
                    updates(b, 9, 10)
                    m_to_rows(b + 1, 0)
                    updates(b, 10, 11)
                    scores(b + 2)
                    updates(b, 11, 12)
                    m_to_rows(b + 1, 1)
                    updates(b, 12, 13)
                    m_to_rows(b + 1, 2)
                    updates(b, 13, C)
                else:
                    updates(b, 4, 8)
                    for j in range(OJ):
                        m_to_rows(b + 1, j)
                        updates(b, 8 + 2 * j, 10 + 2 * j)
            updates(LAST, 0, C)

        @block.scalar
        def _(act):
            def quarters(b):
                act.wait_ge(bx_mm, b + 1)
                if not (isinstance(b, int) and b == 0):
                    act.wait_ge(x_mm, b + 0)
                nc.scalar.copy(x_quarters[:, :], bx_ps[:, :]).then_inc(quarters_done, 1)

            def x_parts_1(b):
                act.wait_ge(x_mm, b + 1)
                if not (isinstance(b, int) and b == 0):
                    act.wait_ge(x_rows_done, b + 0)
                    act.wait_ge(scores_mm, b + 0)
                nc.scalar.activation(x_part1[:, :], x_row_ps[:, :], ACT.Copy,
                                     accum_out=x_sum[:, :]).then_inc(x1_done, 1)
                act.wait_ge(x1_done, b + 1)
                nc.scalar.mul(sum_wide[:, :], ones[:, :], x_sum[0:R, :]).then_inc(wide_done, 1)

            def x_parts_2(b):
                act.wait_ge(xl_done, b + 1)
                nc.scalar.copy(x_part2[:, :], x_left[:, :]).then_inc(x2_done, 1)

            def exponentials(b):
                act.wait_ge(dif_done, b + 1)
                nc.scalar.activation(sexp[:, :], sdif[:, :], ACT.Exp, scale=SCORE_SCALE).then_inc(exp_done, 1)

            def m_parts(b):
                act.wait_ge(m_sum_done, b + 1)
                nc.scalar.copy(m_part[0][:, :], m_left[:, :]).then_inc(m1_done, 1)
                act.wait_ge(ml_done, b + 1)
                nc.scalar.copy(m_part[1][:, :], m_left[:, :]).then_inc(m2_done, 1)

            def m_from_rows(b, first, end):
                for j in range(first, end):
                    act.wait_ge(m_rows_mm, b * OJ + j + 1)
                    nc.scalar.copy(m_rows[:, bass.ds(b % 2, 1), j * S:(j + 1) * S].rearrange("p b m -> p (b m)"),
                                   m_row_ps[:, :]).then_inc(m_rows_done, 1)

            def copy_p(j):
                for g in range(PAIRS):
                    nc.scalar.copy(pw[TILE * j:TILE * (j + 1), g, :],
                                   p_ps[j][TILE * g:TILE * (g + 1), :]).then_inc(pw_act, 1)

            quarters(0)
            act.wait_ge(ones_set, 1)
            act.wait_ge(w_used, C)
            x_parts_1(0)
            copy_p(0)
            exponentials(0)
            x_parts_2(0)
            copy_p(1)
            with act.Fori(0, LAST) as b:
                m_parts(b)
                quarters(b + 1)
                x_parts_1(b + 1)
                m_from_rows(b, 0, 1)
                exponentials(b + 1)
                m_from_rows(b, 1, 3)
                x_parts_2(b + 1)
                m_from_rows(b, 3, 4)
            m_parts(LAST)
            m_from_rows(LAST, 0, OJ)

        @block.vector
        def _(dve):
            def x_less_part1(b):
                dve.wait_ge(x1_done, b + 1)
                nc.vector.scalar_tensor_tensor(x_left[:, :], x_part1[:, :], less_sb[:, 0:1], x_row_ps[:, :],
                                               ALU.mult, ALU.add).then_inc(xl_done, 1)

            def x_less_part2(b):
                dve.wait_ge(x2_done, b + 1)
                nc.vector.scalar_tensor_tensor(x_rows_of(b), x_part2[:, :], less_sb[:, 1:2], x_left[:, :],
                                               ALU.mult, ALU.add).then_inc(x_rows_done, 1)

            def score_differences(b):
                dve.wait_ge(scores_mm, b + 1)
                nc.vector.reduce_max(smax[:, :], m_ps[:, 0:E], AX.X).then_inc(max_done, 1)
                dve.wait_ge(max_done, b + 1)
                nc.vector.tensor_tensor(sdif[:, :], m_ps[:, 0:E], smax[:, :].broadcast_to([P, E]),
                                        ALU.subtract).then_inc(dif_done, 1)

            def coefficients(b):
                dve.wait_ge(exp_done, b + 1)
                nc.vector.reduce_sum(ssum[:, :], sexp[:, :], AX.X).then_inc(sum_done, 1)
                dve.wait_ge(sum_done, b + 1)
                nc.vector.reciprocal(srec[:, :], ssum[:, :]).then_inc(rec_done, 1)
                dve.wait_ge(rec_done, b + 1)
                nc.vector.tensor_tensor(coef[:, :], sexp[:, :], srec[:, :].broadcast_to([P, E]),
                                        ALU.mult).then_inc(coef_done, 1)
                dve.wait_ge(coef_done, b + 1)
                ce = coef[:, :].rearrange("p (k h) -> p k h", h=2)
                for h in range(2):
                    half = slice(h * P // 2, (h + 1) * P // 2)
                    nc.vector.tensor_tensor(g_scaled[half, :, bass.ds(b % 2 * R, R)],
                                            gt[half, :, bass.ds(b * R, R)],
                                            ce[half, :, h].unsqueeze(2).broadcast_to([P // 2, KE, R]),
                                            ALU.mult).then_inc(g_scaled_done, 1)

            def m_sum(b):
                dve.wait_ge(delta_mm, b + 1)
                nc.vector.tensor_tensor(m_left[:, :], m_ps[:, :],
                                        pw[:, bass.ds(b // 2, 1), :].rearrange("p g t -> p (g t)"),
                                        ALU.add).then_inc(m_sum_done, 1)

            def m_less_part1(b):
                dve.wait_ge(m1_done, b + 1)
                nc.vector.tensor_tensor(m_left[:, :], m_left[:, :], m_part[0][:, :],
                                        ALU.subtract).then_inc(ml_done, 1)

            def m_part3(b):
                dve.wait_ge(m2_done, b + 1)
                nc.vector.tensor_tensor(m_part[2][:, :], m_left[:, :], m_part[1][:, :],
                                        ALU.subtract).then_inc(m3_done, 1)

            def add_updates(b, first, end):
                for c in range(first, end):
                    dve.wait_ge(y_mm, b * C + c + 1)
                    nc.vector.tensor_tensor(chunks(b, c), y_ps[c % NY][:, :], chunks(b, c),
                                            ALU.add).then_inc(y_added, 1)

            nc.vector.memset(ones[:, :], 1.0).then_inc(ones_set, 1)
            nc.vector.memset(bx_ps[:, :], 0.0).then_inc(bx_cleared, 1)
            nc.vector.memset(g_scaled[:, :, :], 0.0).then_inc(g_cleared, 1)
            dve.wait_ge(a_in, 16 * NB)
            for k in range(XP):
                cs = slice(k * XC, (k + 1) * XC)
                nc.vector.tensor_copy(a_ord[:, cs, :].rearrange("p c (b r) -> p c b r", b=NB),
                                      a_raw[:, :, cs, :].rearrange("p b c r -> p c b r")).then_inc(a_ordered, 1)
            dve.wait_ge(w_used, C)
            nc.vector.tensor_copy(wat_sb[:, :], wat_ps[:, 0:NB * R]).then_inc(wat_copied, 1)
            nc.vector.tensor_copy(m_left[:, :], g_ps[:, :]).then_inc(g_copied, 1)
            dve.wait_ge(const_in, 16 * 2)
            x_less_part1(0)
            dve.wait_ge(ka_mm, 1)
            nc.vector.tensor_copy(ka[:, :, :].rearrange("r b e -> r (b e)"),
                                  wat_ps[0:R, 0:NB * E]).then_inc(ka_copied, 1)
            dve.wait_ge(gt_mm, 1)
            nc.vector.tensor_copy(gt[:, :, :].rearrange("p k m -> p (k m)"), g_ps[:, :]).then_inc(gt_copied, 1)
            score_differences(0)
            dve.wait_ge(gt_copied, 1)
            dve.wait_ge(g_cleared, 1)
            coefficients(0)
            x_less_part2(0)
            for j in range(OJ // 2, OJ):
                for g in range(PAIRS):
                    nc.vector.tensor_copy(pw[TILE * j:TILE * (j + 1), g, :],
                                          p_ps[j][TILE * g:TILE * (g + 1), :]).then_inc(pw_dve, 1)
            dve.wait_ge(pw_act, 2 * PAIRS)
            dve.wait_ge(pw_dve, 2 * PAIRS)
            m_sum(0)
            m_less_part1(0)
            m_part3(0)
            x_less_part1(1)
            score_differences(1)
            coefficients(1)
            x_less_part2(1)

            def add_and_prepare(b, bx_too):
                add_updates(b, 0, 3)
                m_sum(b + 1)
                add_updates(b, 3, 4)
                m_less_part1(b + 1)
                add_updates(b, 4, 5)
                m_part3(b + 1)
                add_updates(b, 5, 10)
                if bx_too:
                    x_less_part1(b + 2)
                add_updates(b, 10, 11)
                if bx_too:
                    score_differences(b + 2)
                add_updates(b, 11, 12)
                if bx_too:
                    coefficients(b + 2)
                add_updates(b, 12, 15)
                if bx_too:
                    x_less_part2(b + 2)
                add_updates(b, 15, C)

            with dve.Fori(0, LAST - 1) as b:
                add_and_prepare(b, True)
            add_and_prepare(LAST - 1, False)
            add_updates(LAST, 0, C)


def kernel(**inputs):
    import numpy as np
    import ml_dtypes
    import concourse.bacc as bacc
    from concourse.bass_utils import run_bass_kernel_spmd

    x = np.asarray(inputs["x"])
    ids = np.asarray(inputs["itok_B_3_7"])
    A = np.asarray(inputs["L0_cond_A"])
    B = np.asarray(inputs["L0_cond_B"])
    W = np.asarray(inputs["L0_ffn_W_org"])
    down = np.asarray(inputs["L0_ffn_lora_down"])
    up = np.asarray(inputs["L0_ffn_lora_up"])
    keys = np.asarray(inputs["L0_ffn_lora_keys"])
    Wq = np.asarray(inputs["L0_ffn_Wq"])
    NB, S, D = x.shape
    NA, R = A.shape[0], A.shape[2]
    C = D // P
    XP = 4
    E, _, RE = down.shape

    def by_chunk(t):
        return t.reshape(C, P, -1)

    consts = np.zeros((P, 2 * P + 2 + E), np.float32)
    sum_x, less = consts[:, P:2 * P], consts[:, 2 * P:2 * P + 2]
    consts[:, 0:P] = np.eye(P)
    consts[:, 2 * P + 2:] = keys.T
    sel_m = np.zeros((P, 3, 2, P), ml_dtypes.bfloat16)
    for s, (mp, xp) in enumerate(PRODUCTS):
        for r in range(R):
            row = s * R + r
            sum_x[r::TILE, row] = 1
            less[row, 0] = -1 if xp > 0 else 0
            less[row, 1] = -1 if xp > 1 else 0
            for i in range(2):
                sel_m[i * R + r::TILE, mp, i, row] = 1

    arrays = {
        "x": x.reshape(NB, S, XP, C // XP, P).transpose(0, 2, 4, 3, 1),
        "ids": ids.reshape(1, NB),
        "a_tab": A.reshape(NA, C, P, R).transpose(0, 2, 1, 3),
        "b_tab": B.reshape(NA, R, C, P).transpose(0, 3, 2, 1),
        "w_cat": np.concatenate([by_chunk(W.T), by_chunk(down.transpose(1, 0, 2).reshape(D, E * RE)),
                                 by_chunk(Wq.T)], axis=2),
        "up": up.reshape(E * RE // P, P, D).transpose(1, 0, 2),
        "consts": consts,
        "sel_m": sel_m,
    }
    nc = bacc.Bacc("TRN2", target_bir_lowering=False, num_devices=1, dynamic_dma_scratch_size=1024)
    args = {}
    for name in arrays:
        arrays[name] = np.ascontiguousarray(arrays[name])
        args[name] = nc.dram_tensor(f"in_{name}", arrays[name].shape,
                                    mybir.dt.from_np(arrays[name].dtype), kind="ExternalInput").ap()
    out = nc.dram_tensor("out_y", arrays["x"].shape, F32, kind="ExternalOutput").ap()
    lora_ffn(nc, *args.values(), out)
    r = run_bass_kernel_spmd(nc, [{f"in_{n}": a for n, a in arrays.items()}], core_ids=[0])
    y = r.results[0]["out_y"]
    return y.transpose(0, 4, 1, 3, 2).reshape(NB, S, D)
```
